# Optimizing a Trainium2 kernel written in Bass

```python
import numpy as np
import jax
import jax.numpy as jnp

def _softmax(x, axis=-1):
    return jax.nn.softmax(x, axis=axis)

def _gelu(x):
    return jax.nn.gelu(x, approximate=True)

def _silu(x):
    return jax.nn.silu(x)

def _sigmoid(x):
    return jax.nn.sigmoid(x)

def _layernorm(x, axis=-1, eps=1e-05):
    m = jnp.mean(x, axis=axis, keepdims=True)
    v = jnp.var(x, axis=axis, keepdims=True)
    return (x - m) / jnp.sqrt(v + eps)

def _scatter_add(tgt, idx, src, axis=0):
    return tgt.at[idx].add(src)

def _segment_sum(src, seg, n):
    return jax.ops.segment_sum(src, seg, n)
kernel_name = 'mk_dlrm_tower_d1_rec_r8_ea8353'

def setup_inputs(seed: int=0):
    np.random.seed(seed)
    _w = jnp.asarray

    def _rec_inputs():
        import jax
        import jax.numpy as jnp
        _tk = jax.random.key(seed)
        ids = jnp.stack([jax.random.randint(jax.random.fold_in(_tk, 200 + f), (2048,), 0, v, jnp.int32) for f, v in enumerate([1000, 1250, 1250, 1250, 1250, 1000, 1250, 1000, 1250, 125000, 12500, 1000, 1250, 1000, 1000, 1000, 12500, 1250, 1000, 12500, 1250, 12500, 1250, 1000, 12500, 1000])], axis=1)
        tbl_0 = 0.05 * jax.random.normal(jax.random.fold_in(_tk, 500 + 0), (1000, 128), jnp.float32)
        tbl_1 = 0.05 * jax.random.normal(jax.random.fold_in(_tk, 500 + 1), (1250, 128), jnp.float32)
        tbl_2 = 0.05 * jax.random.normal(jax.random.fold_in(_tk, 500 + 2), (1250, 128), jnp.float32)
        tbl_3 = 0.05 * jax.random.normal(jax.random.fold_in(_tk, 500 + 3), (1250, 128), jnp.float32)
        tbl_4 = 0.05 * jax.random.normal(jax.random.fold_in(_tk, 500 + 4), (1250, 128), jnp.float32)
        tbl_5 = 0.05 * jax.random.normal(jax.random.fold_in(_tk, 500 + 5), (1000, 128), jnp.float32)
        tbl_6 = 0.05 * jax.random.normal(jax.random.fold_in(_tk, 500 + 6), (1250, 128), jnp.float32)
        tbl_7 = 0.05 * jax.random.normal(jax.random.fold_in(_tk, 500 + 7), (1000, 128), jnp.float32)
        tbl_8 = 0.05 * jax.random.normal(jax.random.fold_in(_tk, 500 + 8), (1250, 128), jnp.float32)
        tbl_9 = 0.05 * jax.random.normal(jax.random.fold_in(_tk, 500 + 9), (125000, 128), jnp.float32)
        tbl_10 = 0.05 * jax.random.normal(jax.random.fold_in(_tk, 500 + 10), (12500, 128), jnp.float32)
        tbl_11 = 0.05 * jax.random.normal(jax.random.fold_in(_tk, 500 + 11), (1000, 128), jnp.float32)
        tbl_12 = 0.05 * jax.random.normal(jax.random.fold_in(_tk, 500 + 12), (1250, 128), jnp.float32)
        tbl_13 = 0.05 * jax.random.normal(jax.random.fold_in(_tk, 500 + 13), (1000, 128), jnp.float32)
        tbl_14 = 0.05 * jax.random.normal(jax.random.fold_in(_tk, 500 + 14), (1000, 128), jnp.float32)
        tbl_15 = 0.05 * jax.random.normal(jax.random.fold_in(_tk, 500 + 15), (1000, 128), jnp.float32)
        tbl_16 = 0.05 * jax.random.normal(jax.random.fold_in(_tk, 500 + 16), (12500, 128), jnp.float32)
        tbl_17 = 0.05 * jax.random.normal(jax.random.fold_in(_tk, 500 + 17), (1250, 128), jnp.float32)
        tbl_18 = 0.05 * jax.random.normal(jax.random.fold_in(_tk, 500 + 18), (1000, 128), jnp.float32)
        tbl_19 = 0.05 * jax.random.normal(jax.random.fold_in(_tk, 500 + 19), (12500, 128), jnp.float32)
        tbl_20 = 0.05 * jax.random.normal(jax.random.fold_in(_tk, 500 + 20), (1250, 128), jnp.float32)
        tbl_21 = 0.05 * jax.random.normal(jax.random.fold_in(_tk, 500 + 21), (12500, 128), jnp.float32)
        tbl_22 = 0.05 * jax.random.normal(jax.random.fold_in(_tk, 500 + 22), (1250, 128), jnp.float32)
        tbl_23 = 0.05 * jax.random.normal(jax.random.fold_in(_tk, 500 + 23), (1000, 128), jnp.float32)
        tbl_24 = 0.05 * jax.random.normal(jax.random.fold_in(_tk, 500 + 24), (12500, 128), jnp.float32)
        tbl_25 = 0.05 * jax.random.normal(jax.random.fold_in(_tk, 500 + 25), (1000, 128), jnp.float32)
        _rk = jax.random.fold_in(_tk, 7)
        r_bottom_output = -0.000520686 + 1.00062 * jax.random.normal(jax.random.fold_in(_rk, 101), (2048, 128), jnp.float32)
        W_top1 = 0.0456912 * jax.random.normal(jax.random.fold_in(_tk, 801), (479, 512), jnp.float32)
        W_top2 = 0.0441942 * jax.random.normal(jax.random.fold_in(_tk, 802), (512, 256), jnp.float32)
        W_top3 = 0.0625 * jax.random.normal(jax.random.fold_in(_tk, 803), (256, 1), jnp.float32)
        b_top1 = jnp.zeros((512,), jnp.float32)
        b_top2 = jnp.zeros((256,), jnp.float32)
        return (r_bottom_output, ids, tbl_0, tbl_1, tbl_2, tbl_3, tbl_4, tbl_5, tbl_6, tbl_7, tbl_8, tbl_9, tbl_10, tbl_11, tbl_12, tbl_13, tbl_14, tbl_15, tbl_16, tbl_17, tbl_18, tbl_19, tbl_20, tbl_21, tbl_22, tbl_23, tbl_24, tbl_25, W_top1, b_top1, W_top2, b_top2, W_top3)
    r_bottom_output, ids, tbl_0, tbl_1, tbl_2, tbl_3, tbl_4, tbl_5, tbl_6, tbl_7, tbl_8, tbl_9, tbl_10, tbl_11, tbl_12, tbl_13, tbl_14, tbl_15, tbl_16, tbl_17, tbl_18, tbl_19, tbl_20, tbl_21, tbl_22, tbl_23, tbl_24, tbl_25, W_top1, b_top1, W_top2, b_top2, W_top3 = _rec_inputs()

    def _L0_rec_setup():
        import jax, jax.numpy as jnp
        import numpy as np
        NUM_FEATURES = 27
        _TRIU_I, _TRIU_J = np.triu_indices(NUM_FEATURES, k=1)
        key = jax.random.key(seed)
        k1, k2 = jax.random.split(key)
        bottom_output = jax.random.normal(k1, (2048, 128), dtype=jnp.float32)
        embeddings = jax.random.normal(k2, (2048, 26, 128), dtype=jnp.float32)
        return {'bottom_output': bottom_output, 'embeddings': embeddings}
    _L0_rec_all = _L0_rec_setup()
    _L0_rec_in = {k: v for k, v in _L0_rec_all.items() if k in ()}
    del _L0_rec_all
    return {'r_bottom_output': r_bottom_output, 'ids': ids, 'tbl_0': tbl_0, 'tbl_1': tbl_1, 'tbl_2': tbl_2, 'tbl_3': tbl_3, 'tbl_4': tbl_4, 'tbl_5': tbl_5, 'tbl_6': tbl_6, 'tbl_7': tbl_7, 'tbl_8': tbl_8, 'tbl_9': tbl_9, 'tbl_10': tbl_10, 'tbl_11': tbl_11, 'tbl_12': tbl_12, 'tbl_13': tbl_13, 'tbl_14': tbl_14, 'tbl_15': tbl_15, 'tbl_16': tbl_16, 'tbl_17': tbl_17, 'tbl_18': tbl_18, 'tbl_19': tbl_19, 'tbl_20': tbl_20, 'tbl_21': tbl_21, 'tbl_22': tbl_22, 'tbl_23': tbl_23, 'tbl_24': tbl_24, 'tbl_25': tbl_25, 'W_top1': W_top1, 'b_top1': b_top1, 'W_top2': W_top2, 'b_top2': b_top2, 'W_top3': W_top3}

def reference(r_bottom_output, ids, tbl_0, tbl_1, tbl_2, tbl_3, tbl_4, tbl_5, tbl_6, tbl_7, tbl_8, tbl_9, tbl_10, tbl_11, tbl_12, tbl_13, tbl_14, tbl_15, tbl_16, tbl_17, tbl_18, tbl_19, tbl_20, tbl_21, tbl_22, tbl_23, tbl_24, tbl_25, W_top1, b_top1, W_top2, b_top2, W_top3):
    import jax
    import jax.numpy as jnp

    def _L0_rec_ref(bottom_output, embeddings):
        import jax, jax.numpy as jnp
        import numpy as np
        NUM_FEATURES = 27
        _TRIU_I, _TRIU_J = np.triu_indices(NUM_FEATURES, k=1)
        all_emb = jnp.concatenate([bottom_output[:, None, :], embeddings], axis=1)
        gram = jnp.einsum('bfd,bgd->bfg', all_emb, all_emb)
        return gram[:, _TRIU_I, _TRIU_J]
    e = jnp.stack([tbl_0[ids[:, 0]], tbl_1[ids[:, 1]], tbl_2[ids[:, 2]], tbl_3[ids[:, 3]], tbl_4[ids[:, 4]], tbl_5[ids[:, 5]], tbl_6[ids[:, 6]], tbl_7[ids[:, 7]], tbl_8[ids[:, 8]], tbl_9[ids[:, 9]], tbl_10[ids[:, 10]], tbl_11[ids[:, 11]], tbl_12[ids[:, 12]], tbl_13[ids[:, 13]], tbl_14[ids[:, 14]], tbl_15[ids[:, 15]], tbl_16[ids[:, 16]], tbl_17[ids[:, 17]], tbl_18[ids[:, 18]], tbl_19[ids[:, 19]], tbl_20[ids[:, 20]], tbl_21[ids[:, 21]], tbl_22[ids[:, 22]], tbl_23[ids[:, 23]], tbl_24[ids[:, 24]], tbl_25[ids[:, 25]]], axis=1)
    z = _L0_rec_ref(r_bottom_output, e)
    z = z.reshape(z.shape[0], -1)
    h = jnp.concatenate([z, r_bottom_output], axis=1)
    h = jnp.maximum(h @ W_top1 + b_top1, 0.0)
    h = jnp.maximum(h @ W_top2 + b_top2, 0.0)
    y = h @ W_top3
    return y

_drawn_inputs = setup_inputs


def setup_inputs(seed=0):
    import zlib

    import numpy as np

    out = dict(_drawn_inputs(seed))
    spreads = {'b_top1': (0.0, 0.1), 'b_top2': (0.0, 0.1)}
    factors = {}
    for name, (base, spread) in spreads.items():
        noise = np.random.default_rng([zlib.crc32(name.encode()), seed]).standard_normal(out[name].shape)
        drawn = base * np.exp(spread * noise) if base else spread * noise
        out[name] = jnp.asarray(drawn.astype(out[name].dtype))
    for name, factor in factors.items():
        out[name] = (out[name] * factor).astype(out[name].dtype)
    return out
```

```python
from contextlib import ExitStack

import numpy as np
import concourse.bass as bass
from concourse import mybir

F32 = mybir.dt.float32
F16 = mybir.dt.float16
BF16 = mybir.dt.bfloat16
I32 = mybir.dt.int32
ALU = mybir.AluOpType
ACT = mybir.ActivationFunctionType

P = 128
BATCH = 2048
D = 128
NTAB = 26
NF = NTAB + 1
FP = 32
TILES = BATCH // P
TB = 2
BLOCKS = TILES // TB
NB = TB * P
S = 4
Q = P // S
QB = TB * Q
UQ = 8
UNITS = Q // UQ
K = (NF - 1) // 2
FC = 9
PC = FC * K
NC = NF // FC
GW = NF + K
H1, H2 = 512, 256

V = 1000
VP = 125
VC = V // VP
SPLIT = 3

ONEHOT = [0, 5, 7, 11, 13]
X = len(ONEHOT)
GATHERED = [f for f in range(NTAB) if f not in ONEHOT]
NG = len(GATHERED)
ORDER = [0] + [f + 1 for f in GATHERED] + [f + 1 for f in ONEHOT]


def cut(total, sizes):
    out, at = [], 0
    for n in sizes:
        out.append(range(at, at + n))
        at += n
    assert at == total
    return out


ROWS = cut(NG + 1, [4] * (NG // 4) + [NG + 1 - 4 * (NG // 4)])
PICKS = [range(NG + 1 + r.start, NG + 1 + r.stop) for r in cut(X, [4, X - 4])]
SEQUENCE = [("pick", 0), ("rows", 0), ("rows", 1), ("pick", 1)] + [("rows", k) for k in range(2, len(ROWS))]
GROUPS = len(SEQUENCE)
assert GROUPS % 2 == 0
MLP = 7


def pair_rows():
    rows = []
    for f in range(NF):
        for k in range(1, K + 1):
            a, b = sorted((ORDER[f], ORDER[(f + k) % NF]))
            rows.append(a * NF - a * (a + 1) // 2 + b - a - 1)
    return rows


def wait(eng, sem, value):
    if isinstance(value, int) and value <= 0:
        return
    eng.wait_ge(sem, value)


def tower(nc, bottom, idx_rows, idx_cols, tables, w1p, w1b, b1, w2, b2, w3, consts, out):
    with ExitStack() as ctx:
        def sb(name, shape, dt=F32):
            return ctx.enter_context(nc.sbuf_tensor(name, shape, dt))

        def sem(name):
            return ctx.enter_context(nc.semaphore(name))

        const = sb("const", [P, P + VC])
        ident = const[:, 0:P]
        w1p_sb = sb("w1p_sb", [PC, NC, H1])
        w1b_sb = sb("w1b_sb", [P, H1])
        w2_sb = sb("w2_sb", [P, H1 // P, H2])
        w3_sb = sb("w3_sb", [P, H2 // P])
        b1_sb = sb("b1_sb", [P, H1 // P])
        b2_sb = sb("b2_sb", [P, H2 // P])
        parts = sb("parts", [VP, X, SPLIT, VC, D], BF16)
        raw = [sb(f"raw{n}", [VP, VC, D]) for n in range(2)]

        idx = [sb(f"idx{t}", [P, NG], I32) for t in range(TB)]
        rows = [sb(f"rows{t}", [P, NG + 1, D]) for t in range(TB)]
        ids32 = [sb(f"ids32_{t}", [P, X * P], I32) for t in range(TB)]
        ids16 = [sb(f"ids16_{t}", [P, X * P], F16) for t in range(TB)]
        onehot = [sb(f"onehot{t}", [VP, VC, X * P], BF16) for t in range(TB)]
        feat = [sb(f"feat{t}", [P, Q, S, FP]) for t in range(TB)]

        gram = sb("gram", [P, NF, QB])
        pairs = sb("pairs", [PC, NC, NB])
        botT = sb("botT", [P, S, TB, Q])
        h1 = sb("h1", [P, H1 // P, NB])
        h2 = sb("h2", [P, H2 // P, NB])
        y = sb("y", [1, BLOCKS, NB])
        scratch = nc.dram_tensor("scratch", (BLOCKS, FP, GW, S, QB), F32, kind="Internal").ap()

        turn_ps = ctx.enter_context(nc.psum_tensor("turn_ps", [P, 2, 4, P], F32))
        gram_ps = ctx.enter_context(nc.psum_tensor("gram_ps", [P, 2, UQ, P], F32))
        mlp_ps = ctx.enter_context(nc.psum_tensor("mlp_ps", [P, 2, 512], F32))

        const_in = sem("const_in")
        weights_in = sem("weights_in")
        raw_in = [sem(f"raw_in{n}") for n in range(2)]
        part_hi = sem("part_hi")
        rest_hi = sem("rest_hi")
        part_mid = sem("part_mid")
        part_lo = sem("part_lo")
        pad_zero = sem("pad_zero")
        idx_in = [sem(f"idx_in{t}") for t in range(TB)]
        bottom_in = [sem(f"bottom_in{t}") for t in range(TB)]
        ids_in = [sem(f"ids_in{t}") for t in range(TB)]
        gathered = [[sem(f"gathered{t}_{k}") for k in range(len(ROWS))] for t in range(TB)]
        tile_open = sem("tile_open")
        group_done = sem("group_done")
        group_out = sem("group_out")
        ids_fp16 = sem("ids_fp16")
        onehot_done = sem("onehot_done")
        unit_done = sem("unit_done")
        unit_out = sem("unit_out")
        gram_stored = sem("gram_stored")
        pairs_in = sem("pairs_in")
        bot_done = sem("bot_done")
        mlp_done = sem("mlp_done")
        mlp_out = sem("mlp_out")
        y_stored = sem("y_stored")

        block = ctx.enter_context(nc.Block())

        @block.sync
        def _(sp):
            def load_tile(T, t):
                wait(sp, group_done, GROUPS * (T - 1))
                sp.dma_start(idx[t][:, :], idx_rows[T]).then_inc(idx_in[t], 16)
                sp.dma_start(rows[t][:, 0, :], bottom[T]).then_inc(bottom_in[t], 16)
                wait(sp, ids_fp16, T - 1)
                sp.dma_start(ids32[t][:, :], idx_cols[T].to_broadcast((P, X * P))).then_inc(ids_in[t], 16)

            def turn_gram(b):
                sp.wait_ge(unit_out, TB * UNITS * (b + 1))
                for s in range(S):
                    src = gram[s * FP:(s + 1) * FP, :, :]
                    sp.dma_start(scratch[b, :, 0:NF, s, :], src).then_inc(gram_stored, 16)
                    sp.dma_start(scratch[b, :, NF:GW, s, :], src[:, 0:K, :]).then_inc(gram_stored, 16)
                sp.wait_ge(gram_stored, 2 * S * 16 * (b + 1))
                sp.wait_ge(bot_done, b + 1)
                flat = scratch[b].rearrange("f g s q -> (f g) (s q)")
                for c in range(NC):
                    at = FC * c * (GW + 1) + 1
                    src = flat[at:at + FC * (GW + 1), :].rearrange("(f g) n -> f g n", g=GW + 1)[:, 0:K, :]
                    sp.dma_start(pairs[:, c, :], src).then_inc(pairs_in, 16)

            def store_y(first, end):
                sp.wait_ge(mlp_out, MLP * end)
                sp.dma_start(out[:, first:end, :], y[:, first:end, :]).then_inc(y_stored, 16)

            sp.dma_start(const[:, :], consts).then_inc(const_in, 16)
            load_tile(0, 0)

            def load_raw(x):
                wait(sp, part_lo, x - 1)
                sp.dma_start(raw[x % 2][:, :, :], tables[ONEHOT[x]].rearrange("(c p) d -> p c d", p=VP))\
                    .then_inc(raw_in[x % 2], 16)

            load_raw(0)
            load_raw(1)
            load_tile(1, 1)
            for dst, src in ((w1p_sb, w1p), (w1b_sb, w1b), (w2_sb, w2), (w3_sb, w3), (b1_sb, b1), (b2_sb, b2)):
                sp.dma_start(dst[:], src).then_inc(weights_in, 16)
            for x in range(2, X):
                load_raw(x)

            load_tile(2, 0)
            with sp.Fori(1, BLOCKS - 1) as i:
                load_tile(2 * i + 1, 1)
                turn_gram(i - 1)
                load_tile(2 * i + 2, 0)
            load_tile(TILES - 1, 1)
            turn_gram(BLOCKS - 2)
            turn_gram(BLOCKS - 1)
            store_y(0, BLOCKS - 1)
            store_y(BLOCKS - 1, BLOCKS)
            sp.wait_ge(y_stored, 16 * 2)

        @block.gpsimd
        def _(pool):
            def gather_tile(T, t, use):
                pool.wait_ge(idx_in[t], 16 * (use + 1))
                wait(pool, group_done, GROUPS * (T - 1))
                pool.sem_inc(tile_open, 1)
                for k, group in enumerate(ROWS):
                    for j in group:
                        if j == 0:
                            continue
                        pool.indirect_dma_start(
                            rows[t][:, j, :], None, tables[GATHERED[j - 1]],
                            bass.IndirectOffsetOnAxis(ap=idx[t][:, j - 1:j], axis=0)).then_inc(gathered[t][k], 16)

            for t in range(TB):
                gather_tile(t, t, 0)
            with pool.Fori(1, BLOCKS) as i:
                for t in range(TB):
                    gather_tile(2 * i + t, t, i)

        @block.tensor
        def _(pe):
            def group_slot(T, n):
                wait(pe, group_out, GROUPS * T + n - 1)

            def turn_rows(T, t, use, n, k):
                group_slot(T, n)
                if k == 0:
                    pe.wait_ge(bottom_in[t], 16 * (use + 1))
                loads = len([j for j in ROWS[k] if j])
                pe.wait_ge(gathered[t][k], 16 * loads * (use + 1))
                for a, j in enumerate(ROWS[k]):
                    last = pe.transpose(turn_ps[:, n % 2, a, :], rows[t][:, j, :], ident)
                    if a == len(ROWS[k]) - 1:
                        last.then_inc(group_done, 1)

            def pick_rows(T, t, n, g):
                group_slot(T, n)
                pe.wait_ge(onehot_done, T + 1)
                for a, j in enumerate(PICKS[g]):
                    x = j - NG - 1
                    if isinstance(T, int) and T == 0:
                        pe.wait_ge(part_lo, x + 1)
                    for c in range(VC):
                        for m in range(SPLIT):
                            last = pe.matmul(turn_ps[:, n % 2, a, :], parts[:, x, m, c, :],
                                             onehot[t][:, c, x * P:(x + 1) * P],
                                             start=(c == 0 and m == 0), stop=(c == VC - 1 and m == SPLIT - 1))
                last.then_inc(group_done, 1)

            def gram_unit(T, t, u):
                if u == 0:
                    pe.wait_ge(group_out, GROUPS * (T + 1))
                wait(pe, unit_out, UNITS * T + u - 1)
                for r in range(UQ):
                    q = u * UQ + r
                    last = pe.matmul(gram_ps[:, u % 2, r, 0:S * NF], feat[t][:, q, :, :],
                                     feat[t][:, q, :, 0:NF], start=(r % 4 == 0), stop=True,
                                     skip_group_check=True)
                last.then_inc(unit_done, 1)

            def dense(b, j):
                if j == 0:
                    pe.wait_ge(pairs_in, 16 * NC * (b + 1))
                    pe.wait_ge(bot_done, b + 1)
                    if isinstance(b, int) and b == 0:
                        pe.wait_ge(weights_in, 16 * 6)
                if j >= 2:
                    pe.wait_ge(mlp_out, MLP * b + (1, 2, 4, 4, 6)[j - 2])
                if j < 4:
                    cols = slice(j * P, (j + 1) * P)
                    for c in range(NC):
                        pe.matmul(mlp_ps[:, j % 2, 0:NB], w1p_sb[:, c, cols], pairs[:, c, :],
                                  start=(c == 0), stop=False)
                    last = pe.matmul(mlp_ps[:, j % 2, 0:NB], w1b_sb[:, cols],
                                     botT[:, :, :, :].rearrange("d s t q -> d (s t q)"), start=False, stop=True)
                elif j < 6:
                    cols = slice((j - 4) * P, (j - 3) * P)
                    for c in range(4):
                        last = pe.matmul(mlp_ps[:, j % 2, 0:NB], w2_sb[:, c, cols], h1[:, c, :],
                                         start=(c == 0), stop=(c == 3))
                else:
                    for c in range(2):
                        last = pe.matmul(mlp_ps[0:1, 0, 0:NB], w3_sb[:, c:c + 1], h2[:, c, :],
                                         start=(c == 0), stop=(c == 1))
                last.then_inc(mlp_done, 1)

            def tile_step(T, t, use, before=True, dense_block=None):
                for n, (kind, k) in enumerate(SEQUENCE):
                    if kind == "pick":
                        pick_rows(T, t, n, k)
                    else:
                        turn_rows(T, t, use, n, k)
                    if kind == "rows" and k == 0 and before:
                        for u in range(UNITS):
                            gram_unit(T - 1, 1 - t, u)
                    if dense_block is not None and n in DENSE_AT:
                        for j in DENSE_AT[n]:
                            dense(dense_block, j)

            pe.wait_ge(const_in, 16)
            pe.wait_ge(pad_zero, TB)
            tile_step(0, 0, 0, before=False)
            tile_step(1, 1, 0)
            with pe.Fori(1, BLOCKS) as i:
                tile_step(2 * i, 0, i)
                tile_step(2 * i + 1, 1, i, dense_block=i - 1)
            for u in range(UNITS):
                gram_unit(TILES - 1, 1, u)
            for j in range(MLP):
                dense(BLOCKS - 1, j)

        @block.scalar
        def _(act):
            def group_copy(T, t, b, n):
                kind, k = SEQUENCE[n]
                group = ROWS[k] if kind == "rows" else PICKS[k]
                act.wait_ge(group_done, GROUPS * T + n + 1)
                if n == 0:
                    wait(act, unit_done, UNITS * (T - 1))
                    wait(act, bot_done, b)
                act.activation(feat[t][:, :, :, group.start:group.stop].rearrange("d q s f -> d f s q"),
                               turn_ps[:, n % 2, 0:len(group), :].rearrange("d f (s q) -> d f s q", s=S),
                               ACT.Copy).then_inc(group_out, 1)

            def bottom_copy(b):
                act.wait_ge(group_out, GROUPS * TB * (b + 1))
                for t in range(TB):
                    last = act.activation(botT[:, :, t, :], feat[t][:, :, :, 0].rearrange("d q s -> d s q"), ACT.Copy)
                last.then_inc(bot_done, 1)

            def dense_copy(b, j):
                act.wait_ge(mlp_done, MLP * b + j + 1)
                if j < 4:
                    last = act.activation(h1[:, j, :], mlp_ps[:, j % 2, 0:NB], ACT.Relu, bias=b1_sb[:, j:j + 1])
                elif j < 6:
                    last = act.activation(h2[:, j - 4, :], mlp_ps[:, j % 2, 0:NB], ACT.Relu,
                                          bias=b2_sb[:, j - 4:j - 3])
                else:
                    last = act.activation(y[0:1, b, :].rearrange("p (t s q) -> p s t q", s=S, t=TB),
                                          mlp_ps[0:1, 0, 0:NB].rearrange("p (s t q) -> p s t q", s=S, t=TB), ACT.Copy)
                last.then_inc(mlp_out, 1)

            def tile_step(T, t, b, dense_block=None):
                for n in range(GROUPS):
                    group_copy(T, t, b, n)
                    if dense_block is not None and n in DENSE_AT:
                        for j in DENSE_AT[n]:
                            dense_copy(dense_block, j)

            for x in range(X):
                act.wait_ge(raw_in[x % 2], 16 * (x // 2 + 1))
                act.activation(parts[:, x, 0, :, :], raw[x % 2][:, :, :], ACT.Copy).then_inc(part_hi, 1)
                act.wait_ge(rest_hi, x + 1)
                act.activation(parts[:, x, 1, :, :], raw[x % 2][:, :, :], ACT.Copy).then_inc(part_mid, 1)
            act.wait_ge(weights_in, 16 * 6)
            tile_step(0, 0, 0)
            tile_step(1, 1, 0)
            bottom_copy(0)
            with act.Fori(1, BLOCKS) as i:
                tile_step(2 * i, 0, i)
                tile_step(2 * i + 1, 1, i, dense_block=i - 1)
                bottom_copy(i)
            for j in range(MLP):
                dense_copy(BLOCKS - 1, j)

        @block.vector
        def _(dve):
            def onehots(T, t, use):
                dve.wait_ge(ids_in[t], 16 * (use + 1))
                dve.tensor_copy(ids16[t][:, :], ids32[t][:, :]).then_inc(ids_fp16, 1)
                dve.wait_ge(ids_fp16, T + 1)
                wait(dve, group_done, GROUPS * (T - 1))
                for c in range(VC):
                    last = dve.tensor_scalar(onehot[t][:, c, :], ids16[t][0:VP, :], const[0:VP, P + c:P + c + 1],
                                             None, ALU.is_equal)
                last.then_inc(onehot_done, 1)

            def gram_copy(T, t):
                if t == 0:
                    wait(dve, gram_stored, S * 16 * T)
                for u in range(UNITS):
                    dve.wait_ge(unit_done, UNITS * T + u + 1)
                    at = t * Q + u * UQ
                    for s in range(S):
                        last = dve.tensor_copy(
                            gram[s * FP:(s + 1) * FP, :, at:at + UQ].rearrange("p g q -> p q g"),
                            gram_ps[s * FP:(s + 1) * FP, u % 2, :, s * NF:(s + 1) * NF])
                    last.then_inc(unit_out, 1)

            for t in range(TB):
                dve.memset(feat[t][:, :, :, NF:FP], 0.0).then_inc(pad_zero, 1)
            dve.wait_ge(const_in, 16)
            for x in range(X):
                dve.wait_ge(part_hi, x + 1)
                dve.tensor_tensor(raw[x % 2][:, :, :], raw[x % 2][:, :, :], parts[:, x, 0, :, :],
                                  ALU.subtract).then_inc(rest_hi, 1)
                dve.wait_ge(part_mid, x + 1)
                dve.wait_ge(rest_hi, x + 1)
                dve.tensor_tensor(parts[:, x, 2, :, :], raw[x % 2][:, :, :], parts[:, x, 1, :, :],
                                  ALU.subtract).then_inc(part_lo, 1)
                if x == 1:
                    onehots(0, 0, 0)
            onehots(1, 1, 0)
            gram_copy(0, 0)
            with dve.Fori(1, BLOCKS) as i:
                onehots(2 * i, 0, i)
                gram_copy(2 * i - 1, 1)
                onehots(2 * i + 1, 1, i)
                gram_copy(2 * i, 0)
            gram_copy(TILES - 1, 1)


DENSE_AT = {3: (0, 1), 4: (2, 3), 5: (4,), 6: (5,), 7: (6,)}


def kernel(**inputs):
    import concourse.bacc as bacc
    from concourse.bass_utils import run_bass_kernel_spmd

    nc = bacc.Bacc("TRN2", target_bir_lowering=False, num_devices=1)
    arrays = {}

    def given(name, a):
        a = np.ascontiguousarray(a)
        arrays[name] = a
        return nc.dram_tensor(name, a.shape, mybir.dt.from_np(a.dtype), kind="ExternalInput").ap()

    ids = np.asarray(inputs["ids"])
    w1 = np.asarray(inputs["W_top1"])
    npairs = NF * K
    bottom = given("bottom", np.asarray(inputs["r_bottom_output"]).reshape(TILES, P, D))
    idx_rows = given("idx_rows", ids[:, GATHERED].reshape(TILES, P, NG))
    idx_cols = given("idx_cols", ids[:, ONEHOT].reshape(TILES, P, X).transpose(0, 2, 1).reshape(TILES, 1, X * P))
    tables = [given(f"tbl_{f}", inputs[f"tbl_{f}"]) for f in range(NTAB)]
    w1p = given("w1p", w1[pair_rows()].reshape(NC, PC, H1).transpose(1, 0, 2))
    w1b = given("w1b", w1[npairs:])
    b1 = given("b1", np.asarray(inputs["b_top1"]).reshape(H1 // P, P).T)
    w2 = given("w2", np.asarray(inputs["W_top2"]).reshape(H1 // P, P, H2).transpose(1, 0, 2))
    b2 = given("b2", np.asarray(inputs["b_top2"]).reshape(H2 // P, P).T)
    w3 = given("w3", np.asarray(inputs["W_top3"]).reshape(H2 // P, P).T)
    consts = np.zeros((P, P + VC), np.float32)
    consts[:, 0:P] = np.eye(P)
    consts[:, P:] = np.arange(P)[:, None] + VP * np.arange(VC)[None, :]
    consts = given("consts", consts)
    out = nc.dram_tensor("out", (1, BLOCKS, NB), F32, kind="ExternalOutput").ap()
    tower(nc, bottom, idx_rows, idx_cols, tables, w1p, w1b, b1, w2, b2, w3, consts, out)
    r = run_bass_kernel_spmd(nc, [arrays], core_ids=[0])
    return r.results[0]["out"].reshape(BATCH, 1)
```

```python
from contextlib import ExitStack

import numpy as np
import concourse.bass as bass
from concourse import mybir

F32 = mybir.dt.float32
F16 = mybir.dt.float16
BF16 = mybir.dt.bfloat16
I32 = mybir.dt.int32
ALU = mybir.AluOpType
ACT = mybir.ActivationFunctionType

P = 128
BATCH = 2048
D = 128
NTAB = 26
NF = NTAB + 1
FP = 32
TILES = BATCH // P
TB = 2
BLOCKS = TILES // TB
NB = TB * P
S = 4
Q = P // S
QB = TB * Q
UQ = 16
UNITS = Q // UQ
K = (NF - 1) // 2
FC = 9
PC = FC * K
NC = NF // FC
GW = NF + K
H1, H2 = 512, 256

V = 1000
VP = 125
VC = V // VP
SPLIT = 3

ONEHOT = [0, 5, 7, 11, 13, 14]
X = len(ONEHOT)
GATHERED = [f for f in range(NTAB) if f not in ONEHOT]
NG = len(GATHERED)
ORDER = [0] + [f + 1 for f in GATHERED] + [f + 1 for f in ONEHOT]


def cut(total, sizes):
    out, at = [], 0
    for n in sizes:
        out.append(range(at, at + n))
        at += n
    assert at == total
    return out


ROWS = cut(NG + 1, [4] * (NG // 4) + [NG + 1 - 4 * (NG // 4)])
PICKS = [range(NG + 1 + r.start, NG + 1 + r.stop) for r in cut(X, [2, 2, X - 4])]
NR = len(ROWS)

STEPS = [("pick", 0, 0), ("gram", 1, 0), ("rows", 0, 0), ("gram", 1, 1), ("rows", 0, 1), ("pick", 0, 1),
         ("rows", 0, 2), ("pick", 0, 2), ("rows", 0, 3), ("pick", 1, 0), ("rows", 0, 4), ("rows", 0, 5),
         ("pick", 1, 1), ("gram", 0, 0), ("rows", 1, 0), ("gram", 0, 1), ("rows", 1, 1), ("dense", 1),
         ("rows", 1, 2), ("pick", 1, 2), ("rows", 1, 3), ("dense", 2), ("rows", 1, 4), ("rows", 1, 5), ("dense", 3)]
GROUP_AT = {step: n for n, step in enumerate(s for s in STEPS if s[0] in ("pick", "rows"))}
GROUPS = len(GROUP_AT)
RING = 3
assert GROUPS % RING == 0
ROWS_END = [GROUP_AT["rows", t, NR - 1] + 1 for t in range(TB)]
PICKS_END = [max(GROUP_AT["pick", t, g] for g in range(len(PICKS))) + 1 for t in range(TB)]
TILE_START = [min(n for s, n in GROUP_AT.items() if s[1] == t) for t in range(TB)]
TILE_END = [max(n for s, n in GROUP_AT.items() if s[1] == t) + 1 for t in range(TB)]
MLP = 7


def pair_rows():
    rows = []
    for f in range(NF):
        for k in range(1, K + 1):
            a, b = sorted((ORDER[f], ORDER[(f + k) % NF]))
            rows.append(a * NF - a * (a + 1) // 2 + b - a - 1)
    return rows


def wait(eng, sem, value):
    if isinstance(value, int) and value <= 0:
        return
    eng.wait_ge(sem, value)


def tower(nc, bottom, idx_rows, idx_cols, tables, w1p, w1b, b1, w2, b2, w3, consts, out):
    with ExitStack() as ctx:
        def sb(name, shape, dt=F32):
            return ctx.enter_context(nc.sbuf_tensor(name, shape, dt))

        def sem(name):
            return ctx.enter_context(nc.semaphore(name))

        const = sb("const", [P, P + VC])
        ident = const[:, 0:P]
        w1p_sb = sb("w1p_sb", [PC, NC, H1])
        w1b_sb = sb("w1b_sb", [P, H1])
        w2_sb = sb("w2_sb", [P, H1 // P, H2])
        w3_sb = sb("w3_sb", [P, H2 // P])
        b1_sb = sb("b1_sb", [P, H1 // P])
        b2_sb = sb("b2_sb", [P, H2 // P])
        parts = sb("parts", [VP, X, SPLIT, VC, D], BF16)
        raw = [sb(f"raw{n}", [VP, VC, D]) for n in range(2)]

        idx = [sb(f"idx{t}", [P, NG], I32) for t in range(TB)]
        rows = [sb(f"rows{t}", [P, NG + 1, D]) for t in range(TB)]
        ids32 = [sb(f"ids32_{t}", [P, X * P], I32) for t in range(TB)]
        ids16 = [sb(f"ids16_{t}", [P, X * P], F16) for t in range(TB)]
        onehot = [sb(f"onehot{t}", [VP, VC, X * P], BF16) for t in range(TB)]
        feat = [sb(f"feat{t}", [P, Q, S, FP]) for t in range(TB)]

        gram = sb("gram", [P, NF, QB])
        pairs = sb("pairs", [PC, NC, S, QB])
        botT = sb("botT", [P, S, TB, Q])
        h1 = sb("h1", [P, H1 // P, NB])
        h2 = sb("h2", [P, H2 // P, NB])
        y = sb("y", [1, BLOCKS, NB])
        scratch = nc.dram_tensor("scratch", (BLOCKS, P, GW, QB), F32, kind="Internal").ap()

        turn_ps = ctx.enter_context(nc.psum_tensor("turn_ps", [P, RING, 4, P], F32))
        gram_ps = ctx.enter_context(nc.psum_tensor("gram_ps", [P, 2, 512], F32))
        mlp_ps = ctx.enter_context(nc.psum_tensor("mlp_ps", [P, 2, 2, NB], F32))

        const_in = sem("const_in")
        weights_in = sem("weights_in")
        raw_in = [sem(f"raw_in{n}") for n in range(2)]
        split = sem("split")
        part_lo = sem("part_lo")
        pad_zero = sem("pad_zero")
        idx_in = [sem(f"idx_in{t}") for t in range(TB)]
        bottom_in = [sem(f"bottom_in{t}") for t in range(TB)]
        ids_in = [sem(f"ids_in{t}") for t in range(TB)]
        gathered = [[sem(f"gathered{t}_{k}") for k in range(len(ROWS))] for t in range(TB)]
        tile_open = sem("tile_open")
        group_done = sem("group_done")
        group_out = sem("group_out")
        ids_fp16 = sem("ids_fp16")
        onehot_done = sem("onehot_done")
        unit_done = sem("unit_done")
        unit_out = sem("unit_out")
        gram_stored = sem("gram_stored")
        pairs_in = [sem(f"pairs_in{c}") for c in range(NC)]
        bot_done = sem("bot_done")
        mlp_done = sem("mlp_done")
        mlp_out = sem("mlp_out")
        y_stored = sem("y_stored")

        block = ctx.enter_context(nc.Block())

        @block.sync
        def _(sp):
            def load_ids(b, t):
                T = TB * b + t
                wait(sp, ids_fp16, T - 1)
                sp.dma_start(ids32[t][:, :], idx_cols[T].to_broadcast((P, X * P))).then_inc(ids_in[t], 16)

            def load_tile(b, t):
                T = TB * b + t
                wait(sp, group_done, GROUPS * (b - 1) + ROWS_END[t])
                sp.dma_start(idx[t][:, :], idx_rows[T]).then_inc(idx_in[t], 16)
                sp.dma_start(rows[t][:, 0, :], bottom[T]).then_inc(bottom_in[t], 16)

            def store_gram(b):
                sp.wait_ge(unit_out, TB * UNITS * (b + 1))
                sp.dma_start(scratch[b, :, 0:NF, :], gram[:, :, :]).then_inc(gram_stored, 16)
                sp.dma_start(scratch[b, :, NF:GW, :], gram[:, 0:K, :]).then_inc(gram_stored, 16)

            def load_pairs(b):
                sp.wait_ge(gram_stored, 2 * 16 * (b + 1))
                sp.wait_ge(bot_done, b + 1)
                for c in range(NC):
                    for s in range(S):
                        flat = scratch[b, s * FP:(s + 1) * FP, :, :].rearrange("f g q -> (f g) q")
                        at = FC * c * (GW + 1) + 1
                        src = flat[at:at + FC * (GW + 1), :].rearrange("(f g) n -> f g n", g=GW + 1)[:, 0:K, :]
                        sp.dma_start(pairs[:, c, s, :], src).then_inc(pairs_in[c], 16)

            def store_y(first, end):
                sp.wait_ge(mlp_out, MLP * end)
                sp.dma_start(out[:, first:end, :], y[:, first:end, :]).then_inc(y_stored, 16)

            def load_raw(x):
                wait(sp, part_lo, x - 1)
                sp.dma_start(raw[x % 2][:, :, :], tables[ONEHOT[x]].rearrange("(c p) d -> p c d", p=VP))\
                    .then_inc(raw_in[x % 2], 16)

            load_tile(0, 0)
            load_ids(0, 0)
            sp.dma_start(const[:, :], consts).then_inc(const_in, 16)
            load_raw(0)
            load_raw(1)
            load_tile(0, 1)
            load_ids(0, 1)
            for x in range(2, X):
                load_raw(x)
            for dst, src in ((w1p_sb, w1p), (w1b_sb, w1b), (w2_sb, w2), (w3_sb, w3), (b1_sb, b1), (b2_sb, b2)):
                sp.dma_start(dst[:], src).then_inc(weights_in, 16)
            load_ids(1, 0)
            load_tile(1, 0)
            with sp.Fori(1, BLOCKS - 1) as i:
                load_ids(i, 1)
                load_tile(i, 1)
                store_gram(i - 1)
                load_ids(i + 1, 0)
                load_pairs(i - 1)
                load_tile(i + 1, 0)
            load_ids(BLOCKS - 1, 1)
            load_tile(BLOCKS - 1, 1)
            store_gram(BLOCKS - 2)
            load_pairs(BLOCKS - 2)
            store_gram(BLOCKS - 1)
            load_pairs(BLOCKS - 1)
            store_y(0, BLOCKS - 1)
            store_y(BLOCKS - 1, BLOCKS)
            sp.wait_ge(y_stored, 16 * 2)

        @block.gpsimd
        def _(pool):
            def gather_tile(b, t):
                pool.wait_ge(idx_in[t], 16 * (b + 1))
                wait(pool, group_done, GROUPS * (b - 1) + ROWS_END[t])
                pool.sem_inc(tile_open, 1)
                for k, group in enumerate(ROWS):
                    for j in group:
                        if j == 0:
                            continue
                        pool.indirect_dma_start(
                            rows[t][:, j, :], None, tables[GATHERED[j - 1]],
                            bass.IndirectOffsetOnAxis(ap=idx[t][:, j - 1:j], axis=0)).then_inc(gathered[t][k], 16)

            for t in range(TB):
                gather_tile(0, t)
            with pool.Fori(1, BLOCKS) as i:
                for t in range(TB):
                    gather_tile(i, t)

        @block.tensor
        def _(pe):
            def group_slot(b, n):
                wait(pe, group_out, GROUPS * b + n - RING + 1)

            def turn_rows(b, t, k):
                n = GROUP_AT["rows", t, k]
                group_slot(b, n)
                if k == 0:
                    pe.wait_ge(bottom_in[t], 16 * (b + 1))
                loads = len([j for j in ROWS[k] if j])
                pe.wait_ge(gathered[t][k], 16 * loads * (b + 1))
                for a, j in enumerate(ROWS[k]):
                    last = pe.transpose(turn_ps[:, n % RING, a, :], rows[t][:, j, :], ident)
                last.then_inc(group_done, 1)

            def pick_rows(b, t, g):
                n = GROUP_AT["pick", t, g]
                group_slot(b, n)
                pe.wait_ge(onehot_done, TB * b + t + 1)
                for a, j in enumerate(PICKS[g]):
                    x = j - NG - 1
                    if isinstance(b, int) and t == 0:
                        pe.wait_ge(part_lo, x + 1)
                    for c in range(VC):
                        for m in range(SPLIT):
                            last = pe.matmul(turn_ps[:, n % RING, a, :], parts[:, x, m, c, :],
                                             onehot[t][:, c, x * P:(x + 1) * P],
                                             start=(c == 0 and m == 0), stop=(c == VC - 1 and m == SPLIT - 1))
                last.then_inc(group_done, 1)

            def gram_unit(b, t, u):
                T = TB * b + t
                if u == 0:
                    pe.wait_ge(group_out, GROUPS * b + TILE_END[t])
                wait(pe, unit_out, UNITS * T + u - 1)
                for r in range(UQ):
                    for s in range(S):
                        last = pe.matmul(gram_ps[s * FP:(s + 1) * FP, u % 2, r * NF:(r + 1) * NF],
                                         feat[t][:, u * UQ + r, s, :], feat[t][:, u * UQ + r, s, 0:NF],
                                         start=(r == 0), stop=True, skip_group_check=True)
                last.then_inc(unit_done, 1)

            def dense(b, layer):
                if layer == 1:
                    pe.wait_ge(bot_done, b + 1)
                    if isinstance(b, int) and b == 0:
                        pe.wait_ge(weights_in, 16 * 6)
                    for j in range(4):
                        pe.matmul(mlp_ps[:, j // 2, j % 2, :], w1b_sb[:, j * P:(j + 1) * P],
                                  botT[:, :, :, :].rearrange("d s t q -> d (s t q)"),
                                  start=(j % 2 == 0), stop=False, skip_group_check=True)
                    for c in range(NC):
                        pe.wait_ge(pairs_in[c], 16 * S * (b + 1))
                        for j in range(4):
                            last = pe.matmul(mlp_ps[:, j // 2, j % 2, :], w1p_sb[:, c, j * P:(j + 1) * P],
                                             pairs[:, c, :, :].rearrange("p s q -> p (s q)"),
                                             start=False, stop=(c == NC - 1), skip_group_check=True)
                            if c == NC - 1:
                                last.then_inc(mlp_done, 1)
                elif layer == 2:
                    for j in range(2):
                        for c in range(4):
                            if j == 0:
                                pe.wait_ge(mlp_out, MLP * b + max(2, c + 1))
                            last = pe.matmul(mlp_ps[:, j, 0, :], w2_sb[:, c, j * P:(j + 1) * P], h1[:, c, :],
                                             start=(c == 0), stop=(c == 3))
                        last.then_inc(mlp_done, 1)
                else:
                    for c in range(2):
                        pe.wait_ge(mlp_out, MLP * b + 5 + c)
                        last = pe.matmul(mlp_ps[0:1, 0, 0, :], w3_sb[:, c:c + 1], h2[:, c, :],
                                         start=(c == 0), stop=(c == 1))
                    last.then_inc(mlp_done, 1)

            def block_steps(b):
                for step in STEPS:
                    if step[0] == "pick":
                        pick_rows(b, *step[1:])
                    elif step[0] == "rows":
                        turn_rows(b, *step[1:])
                    elif step[0] == "gram" and step[1] == 0:
                        gram_unit(b, 0, step[2])
                    elif isinstance(b, int) and b == 0:
                        continue
                    elif step[0] == "gram":
                        gram_unit(b - 1, 1, step[2])
                    else:
                        dense(b - 1, step[1])

            pe.wait_ge(const_in, 16)
            pe.wait_ge(pad_zero, TB)
            block_steps(0)
            with pe.Fori(1, BLOCKS) as i:
                block_steps(i)
            for u in range(UNITS):
                gram_unit(BLOCKS - 1, 1, u)
            for layer in (1, 2, 3):
                dense(BLOCKS - 1, layer)

        @block.scalar
        def _(act):
            def group_copy(b, kind, t, k):
                n = GROUP_AT[kind, t, k]
                group = ROWS[k] if kind == "rows" else PICKS[k]
                act.wait_ge(group_done, GROUPS * b + n + 1)
                if n == TILE_START[t]:
                    wait(act, unit_done, UNITS * (TB * (b - 1) + t + 1))
                    wait(act, bot_done, b)
                act.activation(feat[t][:, :, :, group.start:group.stop].rearrange("d q s f -> d f s q"),
                               turn_ps[:, n % RING, 0:len(group), :].rearrange("d f (s q) -> d f s q", s=S),
                               ACT.Copy).then_inc(group_out, 1)

            def bottom_copy(b):
                act.wait_ge(group_out, GROUPS * (b + 1))
                for t in range(TB):
                    last = act.activation(botT[:, :, t, :], feat[t][:, :, :, 0].rearrange("d q s -> d s q"), ACT.Copy)
                last.then_inc(bot_done, 1)

            def dense_copy(b, layer):
                for j in {1: range(4), 2: range(4, 6), 3: range(6, 7)}[layer]:
                    act.wait_ge(mlp_done, MLP * b + (j // 2 * 2 + 2 if layer == 1 else j + 1))
                    if layer == 1:
                        last = act.activation(h1[:, j, :], mlp_ps[:, j // 2, j % 2, :], ACT.Relu,
                                              bias=b1_sb[:, j:j + 1])
                    elif layer == 2:
                        last = act.activation(h2[:, j - 4, :], mlp_ps[:, j - 4, 0, :], ACT.Relu,
                                              bias=b2_sb[:, j - 4:j - 3])
                    else:
                        last = act.activation(y[0:1, b, :].rearrange("p (t s q) -> p s t q", s=S, t=TB),
                                              mlp_ps[0:1, 0, 0, :].rearrange("p (s t q) -> p s t q", s=S, t=TB),
                                              ACT.Copy)
                    last.then_inc(mlp_out, 1)

            def block_steps(b):
                for step in STEPS:
                    if step[0] in ("pick", "rows"):
                        group_copy(b, *step)
                    elif step[0] == "dense" and not (isinstance(b, int) and b == 0):
                        dense_copy(b - 1, step[1])
                bottom_copy(b)

            block_steps(0)
            act.wait_ge(weights_in, 16 * 6)
            with act.Fori(1, BLOCKS) as i:
                block_steps(i)
            for layer in (1, 2, 3):
                dense_copy(BLOCKS - 1, layer)

        @block.vector
        def _(dve):
            def onehots(b, t):
                dve.wait_ge(ids_in[t], 16 * (b + 1))
                dve.tensor_copy(ids16[t][:, :], ids32[t][:, :]).then_inc(ids_fp16, 1)
                dve.wait_ge(ids_fp16, TB * b + t + 1)
                wait(dve, group_done, GROUPS * (b - 1) + PICKS_END[t])
                for c in range(VC):
                    last = dve.tensor_scalar(onehot[t][:, c, :], ids16[t][0:VP, :], const[0:VP, P + c:P + c + 1],
                                             None, ALU.is_equal)
                last.then_inc(onehot_done, 1)

            def gram_copy(T, t):
                if t == 0:
                    wait(dve, gram_stored, 16 * T)
                for u in range(UNITS):
                    dve.wait_ge(unit_done, UNITS * T + u + 1)
                    at = t * Q + u * UQ
                    dve.tensor_copy(gram[:, :, at:at + UQ].rearrange("p g q -> p q g"),
                                    gram_ps[:, u % 2, 0:UQ * NF].rearrange("p (q g) -> p q g", g=NF))\
                       .then_inc(unit_out, 1)

            for t in range(TB):
                dve.memset(feat[t][:, :, :, NF:FP], 0.0).then_inc(pad_zero, 1)
            dve.wait_ge(const_in, 16)
            onehots(0, 0)
            for x in range(X):
                whole = raw[x % 2]
                dve.wait_ge(raw_in[x % 2], 16 * (x // 2 + 1))
                dve.tensor_copy(parts[:, x, 0, :, :], whole[:, :, :]).then_inc(split, 1)
                dve.wait_ge(split, 3 * x + 1)
                dve.tensor_tensor(whole[:, :, :], whole[:, :, :], parts[:, x, 0, :, :], ALU.subtract)\
                   .then_inc(split, 1)
                dve.wait_ge(split, 3 * x + 2)
                dve.tensor_copy(parts[:, x, 1, :, :], whole[:, :, :]).then_inc(split, 1)
                dve.wait_ge(split, 3 * x + 3)
                dve.tensor_tensor(parts[:, x, 2, :, :], whole[:, :, :], parts[:, x, 1, :, :], ALU.subtract)\
                   .then_inc(part_lo, 1)
            onehots(0, 1)
            gram_copy(0, 0)
            with dve.Fori(1, BLOCKS) as i:
                onehots(i, 0)
                gram_copy(2 * i - 1, 1)
                onehots(i, 1)
                gram_copy(2 * i, 0)
            gram_copy(TILES - 1, 1)


def kernel(**inputs):
    import concourse.bacc as bacc
    from concourse.bass_utils import run_bass_kernel_spmd

    nc = bacc.Bacc("TRN2", target_bir_lowering=False, num_devices=1)
    arrays = {}

    def given(name, a):
        a = np.ascontiguousarray(a)
        arrays[name] = a
        return nc.dram_tensor(name, a.shape, mybir.dt.from_np(a.dtype), kind="ExternalInput").ap()

    ids = np.asarray(inputs["ids"])
    w1 = np.asarray(inputs["W_top1"])
    npairs = NF * K
    bottom = given("bottom", np.asarray(inputs["r_bottom_output"]).reshape(TILES, P, D))
    idx_rows = given("idx_rows", ids[:, GATHERED].reshape(TILES, P, NG))
    idx_cols = given("idx_cols", ids[:, ONEHOT].reshape(TILES, P, X).transpose(0, 2, 1).reshape(TILES, 1, X * P))
    tables = [given(f"tbl_{f}", inputs[f"tbl_{f}"]) for f in range(NTAB)]
    w1p = given("w1p", w1[pair_rows()].reshape(NC, PC, H1).transpose(1, 0, 2))
    w1b = given("w1b", w1[npairs:])
    b1 = given("b1", np.asarray(inputs["b_top1"]).reshape(H1 // P, P).T)
    w2 = given("w2", np.asarray(inputs["W_top2"]).reshape(H1 // P, P, H2).transpose(1, 0, 2))
    b2 = given("b2", np.asarray(inputs["b_top2"]).reshape(H2 // P, P).T)
    w3 = given("w3", np.asarray(inputs["W_top3"]).reshape(H2 // P, P).T)
    consts = np.zeros((P, P + VC), np.float32)
    consts[:, 0:P] = np.eye(P)
    consts[:, P:] = np.arange(P)[:, None] + VP * np.arange(VC)[None, :]
    consts = given("consts", consts)
    out = nc.dram_tensor("out", (1, BLOCKS, NB), F32, kind="ExternalOutput").ap()
    tower(nc, bottom, idx_rows, idx_cols, tables, w1p, w1b, b1, w2, b2, w3, consts, out)
    r = run_bass_kernel_spmd(nc, [arrays], core_ids=[0])
    return r.results[0]["out"].reshape(BATCH, 1)
```

```python
from contextlib import ExitStack

import numpy as np
import concourse.bass as bass
from concourse import mybir

F32 = mybir.dt.float32
F16 = mybir.dt.float16
F32R = mybir.dt.float32r
I32 = mybir.dt.int32
ALU = mybir.AluOpType
ACT = mybir.ActivationFunctionType

P = 128
BATCH = 2048
D = 128
NTAB = 26
NF = NTAB + 1
FP = 32
TILES = BATCH // P
TB = 2
BLOCKS = TILES // TB
NB = TB * P
S = 4
Q = P // S
QB = TB * Q
UQ = 16
UNITS = Q // UQ
K = (NF - 1) // 2
FC = 9
PC = FC * K
NC = NF // FC
GW = NF + K
H1, H2 = 512, 256

V = 1000
VP = 125
VC = V // VP
SPLIT = 2

LATE = BLOCKS - 3

PICKED = [18, 0, 5, 7, 11, 13, 14, 15]
X = len(PICKED)
TABLE_AT = [f for f in range(NTAB) if f not in PICKED] + PICKED
X0 = NF - X
FIRST_PICK = [X0, X0 + 1]
R = max(FIRST_PICK)
ORDER = [0] + [f + 1 for f in TABLE_AT]


def cut(start, sizes, end):
    out = []
    for n in sizes:
        out.append(range(start, start + n))
        start += n
    assert start == end
    return out


ROWS = [cut(0, [4, 4, 4, 4, 2, 1], FIRST_PICK[0]), cut(0, [4, 4, 4, 4, 3, 1], FIRST_PICK[1])]
PICKS = [cut(FIRST_PICK[0], [2, 2, 2, 2], NF), cut(FIRST_PICK[1], [2, 2, 2, 1], NF)]
NR, NP = 6, 4
HOT = 2
assert NP % HOT == 0

STEPS = [("gram", 1, 0), ("rows", 0, 0), ("gram", 1, 1), ("pick", 0), ("rows", 0, 1), ("pick", 1),
         ("rows", 0, 2), ("pick", 2), ("rows", 0, 3), ("pick", 3), ("rows", 0, 4), ("rows", 0, 5),
         ("dense", 0), ("gram", 0, 0), ("rows", 1, 0), ("gram", 0, 1), ("dense", 1), ("rows", 1, 1),
         ("rows", 1, 2), ("dense", 2), ("rows", 1, 3), ("rows", 1, 4), ("rows", 1, 5), ("dense", 3)]
FIRST_STEPS = [s for s in STEPS if s[0] in ("pick", "rows") or s[:2] == ("gram", 0)]
HIGH_AT = {None: (0, 1), ("rows", 0, 0): (2, 3), ("pick", 0): (4, 5), ("pick", 1): (6, 7)}
FIRST_IDS = slice(0, 2 * NB), slice(2 * NB, X * NB)
LAST_STEPS = STEPS[:STEPS.index(("dense", 1)) + 1] + [
    ("bottom", 0), ("rows", 1, 1), ("rows", 1, 2), ("dense", 2), ("rows", 1, 3), ("dense", 3), ("rows", 1, 4),
    ("rows", 1, 5), ("dense", 0, 0)]
GROUP_AT = {step: n for n, step in enumerate(s for s in STEPS if s[0] in ("pick", "rows"))}
GROUPS = len(GROUP_AT)
RING = 4
assert GROUPS % RING == 0
assert list(GROUP_AT) == [s for s in LAST_STEPS if s[0] in ("pick", "rows")]
FEAT_START = [min(GROUP_AT["rows", t, 0], GROUP_AT["pick", 0]) for t in range(TB)]
FEAT_END = [max(GROUP_AT["rows", t, NR - 1], GROUP_AT["pick", NP - 1]) + 1 for t in range(TB)]
ROWS_END = [GROUP_AT["rows", t, NR - 1] + 1 for t in range(TB)]
MLP = 7
RUNS = BLOCKS + 1

POOL_LOADS = [(c, S - 1) for c in range(NC)] + [(NC - 1, S - 2)]
SP_LOADS = [(c, s) for c in range(NC) for s in range(S) if (c, s) not in POOL_LOADS]


def pair_rows():
    rows = []
    for f in range(NF):
        for k in range(1, K + 1):
            a, b = sorted((ORDER[f], ORDER[(f + k) % NF]))
            rows.append(a * NF - a * (a + 1) // 2 + b - a - 1)
    return rows


def wait(eng, sem, value):
    if isinstance(value, int) and value <= 0:
        return
    eng.wait_ge(sem, value)


def tower(nc, bottom, idx_rows, idx_cols, tables, w1p, w1b, b1, w2, b2, w3, consts, out):
    with ExitStack() as ctx:
        def sb(name, shape, dt=F32):
            return ctx.enter_context(nc.sbuf_tensor(name, shape, dt))

        def sem(name):
            return ctx.enter_context(nc.semaphore(name))

        const = sb("const", [P, P + VC])
        ident = const[:, 0:P]
        w1p_sb = sb("w1p_sb", [PC, NC, H1])
        w1b_sb = sb("w1b_sb", [P, H1])
        w2_sb = sb("w2_sb", [P, H1 // P, H2])
        w3_sb = sb("w3_sb", [P, H2 // P])
        b1_sb = sb("b1_sb", [P, H1 // P])
        b2_sb = sb("b2_sb", [P, H2 // P])
        parts = sb("parts", [VP, X, SPLIT, VC, D], F32R)
        raw = sb("raw", [VP, 2, VC, D])

        idx = [sb(f"idx{t}", [P, R - 1], I32) for t in range(TB)]
        rows = [sb(f"rows{t}", [P, R, D]) for t in range(TB)]
        feat = [sb(f"feat{t}", [P, Q, S, FP]) for t in range(TB)]

        ids32 = sb("ids32", [P, X * NB], I32)
        ids16 = sb("ids16", [P, X * NB], F16)
        onehot = [sb(f"onehot{h}", [VP, VC, 2 * NB], F32R) for h in range(HOT)]
        gram = sb("gram", [P, NF, QB])
        gram_last = gram[:, :, :].rearrange("p g q -> p (g q)").rearrange("p (t g q) -> p t g q", t=TB, g=NF)
        pairs = sb("pairs", [PC, NC, S, QB])
        pairs_last = [sb(f"pairs_last{t}", [PC, NC, S, Q]) for t in range(TB)]
        botT = sb("botT", [P, S, TB, Q])
        h1 = sb("h1", [P, H1 // P, NB])
        h2 = sb("h2", [P, H2 // P, NB])
        y = raw[0:1, :, :, :].rearrange("p n c d -> p (n c d)").rearrange("p (b n) -> p b n", b=BLOCKS)
        scratch = nc.dram_tensor("scratch", (BLOCKS - 1, P, GW, QB), F32, kind="Internal").ap()
        scratch_last = nc.dram_tensor("scratch_last", (TB, P, GW, Q), F32, kind="Internal").ap()

        turn_ps = ctx.enter_context(nc.psum_tensor("turn_ps", [P, RING, 4, P], F32))
        gram_ps = ctx.enter_context(nc.psum_tensor("gram_ps", [P, 2, 512], F32))
        mlp_ps = ctx.enter_context(nc.psum_tensor("mlp_ps", [P, 2, 2, NB], F32))

        const_in = sem("const_in")
        weights_in = sem("weights_in")
        raw_in = [sem(f"raw_in{n}") for n in range(2)]
        part_hi = sem("part_hi")
        part_lo = sem("part_lo")
        pad_zero = sem("pad_zero")
        idx_in = [sem(f"idx_in{t}") for t in range(TB)]
        bottom_in = [sem(f"bottom_in{t}") for t in range(TB)]
        ids_in = sem("ids_in")
        gathered = [[sem(f"gathered{t}_{k}") for k in range(NR)] for t in range(TB)]
        tile_open = sem("tile_open")
        group_done = sem("group_done")
        group_out = sem("group_out")
        first_ids_in = sem("first_ids_in")
        first_ids_fp16 = sem("first_ids_fp16")
        ids_fp16 = sem("ids_fp16")
        onehot_done = sem("onehot_done")
        unit_done = sem("unit_done")
        unit_out = sem("unit_out")
        gram_stored = sem("gram_stored")
        pairs_in = [sem(f"pairs_in{c}") for c in range(NC)]
        last_pairs_in = [[sem(f"last_pairs_in{t}_{c}") for c in range(NC)] for t in range(TB)]
        last_pairs_pool = [sem(f"last_pairs_pool{c}") for c in range(NC)]
        bot_done = sem("bot_done")
        mlp_done = sem("mlp_done")
        mlp_out = sem("mlp_out")
        y_stored = sem("y_stored")

        block = ctx.enter_context(nc.Block())

        def pair_rows_of(scratch_of, c, s):
            flat = scratch_of[s * FP:(s + 1) * FP, :, :].rearrange("f g q -> (f g) q")
            at = FC * c * (GW + 1) + 1
            return flat[at:at + FC * (GW + 1), :].rearrange("(f g) n -> f g n", g=GW + 1)[:, 0:K, :]

        def load_last_pairs(eng, loads, loaded):
            eng.wait_ge(gram_stored, 2 * 16 * RUNS)
            for c, s in loads:
                eng.dma_start(pairs_last[TB - 1][:, c, s, :], pair_rows_of(scratch_last[TB - 1], c, s))\
                   .then_inc(loaded[c], 16)

        @block.sync
        def _(sp):
            def load_ids(b):
                wait(sp, ids_fp16, b)
                sp.dma_start(ids32[:, :], idx_cols[b].to_broadcast((P, X * NB))).then_inc(ids_in, 16)

            def load_tile(b, t):
                T = TB * b + t
                wait(sp, group_done, GROUPS * (b - 1) + ROWS_END[t])
                sp.dma_start(idx[t][:, :], idx_rows[T]).then_inc(idx_in[t], 16)
                sp.dma_start(rows[t][:, 0, :], bottom[T]).then_inc(bottom_in[t], 16)

            def store_gram(units, gram_of, scratch_of):
                sp.wait_ge(unit_out, units)
                sp.dma_start(scratch_of[:, 0:NF, :], gram_of).then_inc(gram_stored, 16)
                sp.dma_start(scratch_of[:, NF:GW, :], gram_of[:, 0:K, :]).then_inc(gram_stored, 16)

            def load_pairs(run, pairs_of, scratch_of, bottoms, loaded):
                sp.wait_ge(gram_stored, 2 * 16 * (run + 1))
                wait(sp, bot_done, bottoms)
                for c in range(NC):
                    for s in range(S):
                        sp.dma_start(pairs_of(c, s), pair_rows_of(scratch_of, c, s)).then_inc(loaded[c], 16)

            def store_block(b):
                store_gram(TB * UNITS * (b + 1), gram[:, :, :], scratch[b])

            def load_block(b):
                load_pairs(b, lambda c, s: pairs[:, c, s, :], scratch[b], b + 1, pairs_in)

            def store_y(blocks, samples, runs):
                sp.wait_ge(mlp_out, MLP * runs)
                sp.dma_start(out[:, blocks, samples], y[:, blocks, samples]).then_inc(y_stored, 16)

            def load_raw(n):
                wait(sp, part_lo, n - 1)
                sp.dma_start(raw[:, n % 2, :, :], tables[PICKED[n]].rearrange("(c p) d -> p c d", p=VP))\
                    .then_inc(raw_in[n % 2], 16)

            load_tile(0, 0)
            sp.dma_start(const[:, :], consts).then_inc(const_in, 16)
            for cols, loaded in zip(FIRST_IDS, (first_ids_in, ids_in)):
                sp.dma_start(ids32[:, cols], idx_cols[0][:, cols].to_broadcast((P, cols.stop - cols.start)))\
                  .then_inc(loaded, 16)
            load_raw(0)
            load_raw(1)
            load_tile(0, 1)
            for n in range(2, X):
                load_raw(n)
            for dst, src in ((w1p_sb, w1p), (w1b_sb, w1b), (w2_sb, w2), (w3_sb, w3), (b1_sb, b1), (b2_sb, b2)):
                sp.dma_start(dst[:], src).then_inc(weights_in, 16)
            load_ids(1)
            load_tile(1, 0)
            with sp.Fori(1, BLOCKS - 1) as i:
                load_tile(i, 1)
                store_block(i - 1)
                load_ids(i + 1)
                load_block(i - 1)
                load_tile(i + 1, 0)
            load_tile(BLOCKS - 1, 1)
            store_block(BLOCKS - 2)
            load_block(BLOCKS - 2)
            for t in range(TB):
                store_gram(TB * UNITS * (BLOCKS - 1) + UNITS * (t + 1), gram_last[:, t, :, :], scratch_last[t])
                if t == 0:
                    load_pairs(BLOCKS - 1, lambda c, s: pairs_last[0][:, c, s, :], scratch_last[0], 0,
                               last_pairs_in[0])
            load_last_pairs(sp, SP_LOADS, last_pairs_in[1])
            store_y(slice(0, BLOCKS - 1), slice(0, NB), BLOCKS - 1)
            store_y(slice(BLOCKS - 1, BLOCKS), slice(0, P), BLOCKS)
            store_y(slice(BLOCKS - 1, BLOCKS), slice(P, NB), RUNS)
            sp.wait_ge(y_stored, 16 * 3)

        @block.gpsimd
        def _(pool):
            def gather_tile(b, late, t):
                pool.wait_ge(idx_in[t], 16 * (b + 1))
                wait(pool, group_done, GROUPS * (b - 1) + ROWS_END[t])
                pool.sem_inc(tile_open, 1)
                for k, group in enumerate(ROWS[late]):
                    for j in group:
                        if j == 0:
                            continue
                        pool.indirect_dma_start(
                            rows[t][:, j, :], None, tables[TABLE_AT[j - 1]],
                            bass.IndirectOffsetOnAxis(ap=idx[t][:, j - 1:j], axis=0)).then_inc(gathered[t][k], 16)

            def gather_block(b, late):
                for t in range(TB):
                    gather_tile(b, late, t)

            gather_block(0, 0)
            with pool.Fori(1, LATE) as i:
                gather_block(i, 0)
            with pool.Fori(LATE, BLOCKS) as i:
                gather_block(i, 1)
            load_last_pairs(pool, POOL_LOADS, last_pairs_pool)

        @block.tensor
        def _(pe):
            def group_slot(b, n):
                wait(pe, group_out, GROUPS * b + n - RING + 1)

            def turn_rows(b, late, t, k):
                n = GROUP_AT["rows", t, k]
                group_slot(b, n)
                if k == 0:
                    pe.wait_ge(bottom_in[t], 16 * (b + 1))
                loads = [len([j for j in rows_of[k] if j]) for rows_of in ROWS]
                pe.wait_ge(gathered[t][k], 16 * (loads[1] * (b + 1 - LATE) + loads[0] * LATE if late else
                                                 loads[0] * (b + 1)))
                for a, j in enumerate(ROWS[late][k]):
                    last = pe.transpose(turn_ps[:, n % RING, a, :], rows[t][:, j, :], ident)
                last.then_inc(group_done, 1)

            def pick_rows(b, late, g):
                n = GROUP_AT["pick", g]
                group_slot(b, n)
                pe.wait_ge(onehot_done, NP * b + g + 1)
                for a, j in enumerate(PICKS[late][g]):
                    x = j - X0
                    if isinstance(b, int) and b == 0:
                        pe.wait_ge(part_lo, x + 1)
                    for c in range(VC):
                        for m in range(SPLIT):
                            last = pe.matmul(turn_ps[:, n % RING, 2 * a:2 * a + 2, :], parts[:, x, m, c, :],
                                             onehot[g % HOT][:, c, a * NB:(a + 1) * NB],
                                             start=(c == 0 and m == 0), stop=(c == VC - 1 and m == SPLIT - 1))
                last.then_inc(group_done, 1)

            def gram_unit(b, t, u):
                T = TB * b + t
                if u == 0:
                    pe.wait_ge(group_out, GROUPS * b + FEAT_END[t])
                wait(pe, unit_out, UNITS * T + u - 1)
                for r in range(UQ):
                    for s in range(S):
                        last = pe.matmul(gram_ps[s * FP:(s + 1) * FP, u % 2, r * NF:(r + 1) * NF],
                                         feat[t][:, u * UQ + r, s, :], feat[t][:, u * UQ + r, s, 0:NF],
                                         start=(r == 0), stop=True, skip_group_check=True)
                last.then_inc(unit_done, 1)

            def dense(run, layer, t=None):
                n = NB if t is None else P
                if layer == 0:
                    pe.wait_ge(bot_done, run + 1)
                    if t is not None:
                        pe.wait_ge(mlp_out, MLP * run)
                    bot = botT[:, :, :, :].rearrange("d s t q -> d (s t q)") if t is None else botT[:, :, t, :]
                    for j in range(4):
                        pe.matmul(mlp_ps[:, j // 2, j % 2, 0:n], w1b_sb[:, j * P:(j + 1) * P], bot,
                                  start=(j % 2 == 0), stop=False, skip_group_check=True)
                elif layer == 1:
                    for c in range(NC):
                        if t is None:
                            pe.wait_ge(pairs_in[c], 16 * S * (run + 1))
                        elif t == 0:
                            pe.wait_ge(last_pairs_in[0][c], 16 * S)
                        else:
                            pe.wait_ge(last_pairs_in[1][c], 16 * len([1 for load in SP_LOADS if load[0] == c]))
                            pe.wait_ge(last_pairs_pool[c], 16 * len([1 for load in POOL_LOADS if load[0] == c]))
                        chunk = pairs[:, c, :, :] if t is None else pairs_last[t][:, c, :, :]
                        for j in range(4):
                            last = pe.matmul(mlp_ps[:, j // 2, j % 2, 0:n], w1p_sb[:, c, j * P:(j + 1) * P],
                                             chunk.rearrange("p s q -> p (s q)"),
                                             start=False, stop=(c == NC - 1), skip_group_check=True)
                            if c == NC - 1:
                                last.then_inc(mlp_done, 1)
                elif layer == 2:
                    for j in range(2):
                        for c in range(4):
                            if j == 0:
                                pe.wait_ge(mlp_out, MLP * run + max(2, c + 1))
                            last = pe.matmul(mlp_ps[:, j, 0, 0:n], w2_sb[:, c, j * P:(j + 1) * P], h1[:, c, 0:n],
                                             start=(c == 0), stop=(c == 3))
                        last.then_inc(mlp_done, 1)
                else:
                    for c in range(2):
                        pe.wait_ge(mlp_out, MLP * run + 5 + c)
                        last = pe.matmul(mlp_ps[0:1, 0, 0, 0:n], w3_sb[:, c:c + 1], h2[:, c, 0:n],
                                         start=(c == 0), stop=(c == 1))
                    last.then_inc(mlp_done, 1)

            def block_steps(b, late, steps):
                for kind, *step in steps:
                    if kind == "pick":
                        pick_rows(b, late, *step)
                    elif kind == "rows":
                        turn_rows(b, late, *step)
                    elif kind == "gram":
                        gram_unit(b - step[0], *step)
                    elif kind == "dense":
                        dense(b - 1 if len(step) == 1 else b, *step)

            pe.wait_ge(const_in, 16)
            pe.wait_ge(pad_zero, TB)
            block_steps(0, 0, FIRST_STEPS)
            pe.wait_ge(weights_in, 16 * 6)
            with pe.Fori(1, LATE) as i:
                block_steps(i, 0, STEPS)
            with pe.Fori(LATE, BLOCKS - 1) as i:
                block_steps(i, 1, STEPS)
            block_steps(BLOCKS - 1, 1, LAST_STEPS)
            for u in range(UNITS):
                gram_unit(BLOCKS - 1, 1, u)
            for layer in (1, 2, 3):
                dense(BLOCKS - 1, layer, 0)
            for layer in range(4):
                dense(RUNS - 1, layer, 1)

        @block.scalar
        def _(act):
            def feat_free(b, n, t):
                if n == FEAT_START[t]:
                    wait(act, unit_done, UNITS * (TB * (b - 1) + t + 1))
                    wait(act, bot_done, b)

            def rows_copy(b, late, t, k):
                n, group = GROUP_AT["rows", t, k], ROWS[late][k]
                act.wait_ge(group_done, GROUPS * b + n + 1)
                feat_free(b, n, t)
                act.activation(feat[t][:, :, :, group.start:group.stop].rearrange("d q s f -> d f s q"),
                               turn_ps[:, n % RING, 0:len(group), :].rearrange("d f (s q) -> d f s q", s=S),
                               ACT.Copy).then_inc(group_out, 1)

            def picks_copy(b, late, g):
                n, group = GROUP_AT["pick", g], PICKS[late][g]
                bank = turn_ps[:, n % RING, 0:TB * len(group), :].rearrange("d (f t) n -> d t f n", t=TB)
                act.wait_ge(group_done, GROUPS * b + n + 1)
                for t in range(TB):
                    feat_free(b, n, t)
                    last = act.activation(feat[t][:, :, :, group.start:group.stop].rearrange("d q s f -> d f s q"),
                                          bank[:, t, :, :].rearrange("d f (s q) -> d f s q", s=S), ACT.Copy)
                last.then_inc(group_out, 1)

            def bottom_copy(run, groups, tiles):
                act.wait_ge(group_out, groups)
                for t in tiles:
                    last = act.activation(botT[:, :, t, :], feat[t][:, :, :, 0].rearrange("d q s -> d s q"), ACT.Copy)
                last.then_inc(bot_done, 1)

            def dense_copy(run, layer, t=None):
                n = NB if t is None else P
                for j in {0: (), 1: range(4), 2: range(4, 6), 3: range(6, 7)}[layer]:
                    act.wait_ge(mlp_done, MLP * run + (j // 2 * 2 + 2 if layer == 1 else j + 1))
                    if layer == 1:
                        last = act.activation(h1[:, j, 0:n], mlp_ps[:, j // 2, j % 2, 0:n], ACT.Relu,
                                              bias=b1_sb[:, j:j + 1])
                    elif layer == 2:
                        last = act.activation(h2[:, j - 4, 0:n], mlp_ps[:, j - 4, 0, 0:n], ACT.Relu,
                                              bias=b2_sb[:, j - 4:j - 3])
                    elif t is None:
                        last = act.activation(y[0:1, run, :].rearrange("p (t s q) -> p s t q", s=S, t=TB),
                                              mlp_ps[0:1, 0, 0, :].rearrange("p (s t q) -> p s t q", s=S, t=TB),
                                              ACT.Copy)
                    else:
                        last = act.activation(y[0:1, BLOCKS - 1, t * P:(t + 1) * P], mlp_ps[0:1, 0, 0, 0:P], ACT.Copy)
                    last.then_inc(mlp_out, 1)

            def block_steps(b, late, steps):
                for kind, *step in steps:
                    if kind == "rows":
                        rows_copy(b, late, *step)
                    elif kind == "pick":
                        picks_copy(b, late, *step)
                    elif kind == "dense":
                        dense_copy(b - 1 if len(step) == 1 else b, *step)
                    elif kind == "bottom":
                        bottom_copy(b, GROUPS * b + FEAT_END[0], step)

            def cut_high(n):
                act.wait_ge(raw_in[n % 2], 16 * (n // 2 + 1))
                act.activation(parts[:, n, 0, :, :], raw[:, n % 2, :, :], ACT.Copy).then_inc(part_hi, 1)

            for n in HIGH_AT[None]:
                cut_high(n)
            for step in FIRST_STEPS:
                block_steps(0, 0, [step])
                for n in HIGH_AT.get(step, ()):
                    cut_high(n)
            bottom_copy(0, GROUPS, range(TB))
            act.wait_ge(weights_in, 16 * 6)
            with act.Fori(1, LATE) as i:
                block_steps(i, 0, STEPS)
                bottom_copy(i, GROUPS * (i + 1), range(TB))
            with act.Fori(LATE, BLOCKS - 1) as i:
                block_steps(i, 1, STEPS)
                bottom_copy(i, GROUPS * (i + 1), range(TB))
            block_steps(BLOCKS - 1, 1, LAST_STEPS)
            bottom_copy(RUNS - 1, GROUPS * BLOCKS, (1,))
            for layer in (1, 2, 3):
                dense_copy(BLOCKS - 1, layer, 0)
            for layer in (1, 2, 3):
                dense_copy(RUNS - 1, layer, 1)

        @block.vector
        def _(dve):
            def ids_convert(b):
                dve.wait_ge(ids_in, 16 * (b + 1))
                wait(dve, onehot_done, NP * b)
                dve.tensor_copy(ids16[:, :], ids32[:, :]).then_inc(ids_fp16, 1)

            def onehots(b, late, g):
                group = PICKS[late][g]
                if g or not (isinstance(b, int) and b == 0):
                    dve.wait_ge(ids_fp16, b + 1)
                if g < HOT:
                    wait(dve, group_done, GROUPS * (b - 1) + GROUP_AT["pick", g + NP - HOT] + 1)
                else:
                    dve.wait_ge(group_done, GROUPS * b + GROUP_AT["pick", g - HOT] + 1)
                for c in range(VC):
                    last = dve.tensor_scalar(onehot[g % HOT][:, c, 0:len(group) * NB],
                                             ids16[0:VP, (group.start - X0) * NB:(group.stop - X0) * NB],
                                             const[0:VP, P + c:P + c + 1], None, ALU.is_equal)
                last.then_inc(onehot_done, 1)

            def gram_copy(T, t, gram_of):
                if t == 0:
                    wait(dve, gram_stored, 16 * T)
                for u in range(UNITS):
                    dve.wait_ge(unit_done, UNITS * T + u + 1)
                    dve.tensor_copy(gram_of[:, :, u * UQ:(u + 1) * UQ].rearrange("p g q -> p q g"),
                                    gram_ps[:, u % 2, 0:UQ * NF].rearrange("p (q g) -> p q g", g=NF))\
                       .then_inc(unit_out, 1)

            def cut_low(n):
                dve.wait_ge(part_hi, n + 1)
                dve.tensor_tensor(parts[:, n, 1, :, :], raw[:, n % 2, :, :], parts[:, n, 0, :, :], ALU.subtract)\
                   .then_inc(part_lo, 1)

            def block_steps(b, late, last_tile):
                ids_convert(b)
                for g in range(HOT):
                    onehots(b, late, g)
                gram_copy(2 * b - 1, 1, gram[:, :, Q:QB])
                for g in range(HOT, NP):
                    onehots(b, late, g)
                gram_copy(2 * b, 0, last_tile)

            for t in range(TB):
                dve.memset(feat[t][:, :, :, NF:FP], 0.0).then_inc(pad_zero, 1)
            dve.wait_ge(const_in, 16)
            dve.wait_ge(first_ids_in, 16)
            dve.tensor_copy(ids16[:, FIRST_IDS[0]], ids32[:, FIRST_IDS[0]]).then_inc(first_ids_fp16, 1)
            dve.wait_ge(first_ids_fp16, 1)
            for g in range(NP):
                if g == 1:
                    dve.wait_ge(ids_in, 16)
                    dve.tensor_copy(ids16[:, FIRST_IDS[1]], ids32[:, FIRST_IDS[1]]).then_inc(ids_fp16, 1)
                onehots(0, 0, g)
                for j in PICKS[0][g]:
                    cut_low(j - X0)
            gram_copy(0, 0, gram[:, :, 0:Q])
            with dve.Fori(1, LATE) as i:
                block_steps(i, 0, gram[:, :, 0:Q])
            with dve.Fori(LATE, BLOCKS - 1) as i:
                block_steps(i, 1, gram[:, :, 0:Q])
            block_steps(BLOCKS - 1, 1, gram_last[:, 0, :, :])
            gram_copy(TILES - 1, 1, gram_last[:, 1, :, :])


def kernel(**inputs):
    import concourse.bacc as bacc
    from concourse.bass_utils import run_bass_kernel_spmd

    nc = bacc.Bacc("TRN2", target_bir_lowering=False, num_devices=1)
    arrays = {}

    def given(name, a):
        a = np.ascontiguousarray(a)
        arrays[name] = a
        return nc.dram_tensor(name, a.shape, mybir.dt.from_np(a.dtype), kind="ExternalInput").ap()

    ids = np.asarray(inputs["ids"])
    w1 = np.asarray(inputs["W_top1"])
    npairs = NF * K
    bottom = given("bottom", np.asarray(inputs["r_bottom_output"]).reshape(TILES, P, D))
    idx_rows = given("idx_rows", ids[:, TABLE_AT[:R - 1]].reshape(TILES, P, R - 1))
    idx_cols = given("idx_cols", ids[:, PICKED].reshape(BLOCKS, NB, X).transpose(0, 2, 1).reshape(BLOCKS, 1, X * NB))
    tables = [given(f"tbl_{f}", inputs[f"tbl_{f}"]) for f in range(NTAB)]
    w1p = given("w1p", w1[pair_rows()].reshape(NC, PC, H1).transpose(1, 0, 2))
    w1b = given("w1b", w1[npairs:])
    b1 = given("b1", np.asarray(inputs["b_top1"]).reshape(H1 // P, P).T)
    w2 = given("w2", np.asarray(inputs["W_top2"]).reshape(H1 // P, P, H2).transpose(1, 0, 2))
    b2 = given("b2", np.asarray(inputs["b_top2"]).reshape(H2 // P, P).T)
    w3 = given("w3", np.asarray(inputs["W_top3"]).reshape(H2 // P, P).T)
    consts = np.zeros((P, P + VC), np.float32)
    consts[:, 0:P] = np.eye(P)
    consts[:, P:] = np.arange(P)[:, None] + VP * np.arange(VC)[None, :]
    consts = given("consts", consts)
    out = nc.dram_tensor("out", (1, BLOCKS, NB), F32, kind="ExternalOutput").ap()
    tower(nc, bottom, idx_rows, idx_cols, tables, w1p, w1b, b1, w2, b2, w3, consts, out)
    r = run_bass_kernel_spmd(nc, [arrays], core_ids=[0])
    return r.results[0]["out"].reshape(BATCH, 1)
```
